# Optimizing a Trainium2 kernel written in Bass

```python
import numpy as np
import jax
import jax.numpy as jnp

def _softmax(x, axis=-1):
    return jax.nn.softmax(x, axis=axis)

def _gelu(x):
    return jax.nn.gelu(x, approximate=True)

def _silu(x):
    return jax.nn.silu(x)

def _sigmoid(x):
    return jax.nn.sigmoid(x)

def _layernorm(x, axis=-1, eps=1e-05):
    m = jnp.mean(x, axis=axis, keepdims=True)
    v = jnp.var(x, axis=axis, keepdims=True)
    return (x - m) / jnp.sqrt(v + eps)

def _scatter_add(tgt, idx, src, axis=0):
    return tgt.at[idx].add(src)

def _segment_sum(src, seg, n):
    return jax.ops.segment_sum(src, seg, n)
kernel_name = 'mk_adj_preln_d1_adj_r2_1d6a3f'

def setup_inputs(seed: int=0):
    np.random.seed(seed)
    _w = jnp.asarray

    def _rec_inputs():
        import jax
        import jax.numpy as jnp
        _gk = jax.random.key(seed)
        x = 0.0002141 + 1 * jax.random.normal(jax.random.fold_in(_gk, 1), (8192, 64), jnp.float32)
        _a = jax.random.bernoulli(jax.random.fold_in(_gk, 2), 0.000976562, (8192, 8192))
        _a = jnp.logical_or(_a, jnp.eye(8192, dtype=bool))
        _af = _a.astype(jnp.float32)
        _af = _af * jax.random.uniform(jax.random.fold_in(_gk, 3), (8192, 8192), jnp.float32, 0.05, 1)
        adj = _af
        return (x, adj)
    x, adj = _rec_inputs()

    def _L0_gnn_setup():
        import jax, jax.numpy as jnp
        import numpy as np
        N = 6144
        D_IN = 64
        D_OUT = 64
        BN_EPS = 1e-05
        LEAKY_SLOPE = 0.01

        def _normalize_adj(A):
            n = A.shape[0]
            idx = jnp.arange(n)
            A = A.at[idx, idx].add(1.0)
            d = jax.lax.rsqrt(A.sum(axis=1))
            return d[:, None] * A * d[None, :]
        key = jax.random.key(seed)
        k_h, k_w, k_b, k_a = jax.random.split(key, 4)
        H = jax.random.normal(k_h, (N, D_IN), dtype=jnp.float32)
        W = jax.random.normal(k_w, (D_IN, D_OUT), dtype=jnp.float32) * (1.0 / np.sqrt(D_IN))
        b = jax.random.normal(k_b, (D_OUT,), dtype=jnp.float32) * 0.01
        gamma = jnp.ones((D_OUT,), dtype=jnp.float32)
        beta = jnp.zeros((D_OUT,), dtype=jnp.float32)
        A = jax.random.uniform(k_a, (N, N), dtype=jnp.float32)
        return {'H': H, 'W': W, 'b': b, 'gamma': gamma, 'beta': beta, 'A': A}
    _L0_gnn_all = _L0_gnn_setup()
    _L0_gnn_in = {k: v for k, v in _L0_gnn_all.items() if k in ('W', 'b', 'gamma', 'beta')}
    del _L0_gnn_all
    return {'x': x, 'adj': adj, 'L0_gnn_W': _L0_gnn_in['W'], 'L0_gnn_b': _L0_gnn_in['b'], 'L0_gnn_gamma': _L0_gnn_in['gamma'], 'L0_gnn_beta': _L0_gnn_in['beta']}

def reference(x, adj, L0_gnn_W, L0_gnn_b, L0_gnn_gamma, L0_gnn_beta):
    import jax
    import jax.numpy as jnp

    def _L0_gnn_ref(H, W, b, gamma, beta, A):
        import jax, jax.numpy as jnp
        import numpy as np
        N = 6144
        D_IN = 64
        D_OUT = 64
        BN_EPS = 1e-05
        LEAKY_SLOPE = 0.01

        def _normalize_adj(A):
            n = A.shape[0]
            idx = jnp.arange(n)
            A = A.at[idx, idx].add(1.0)
            d = jax.lax.rsqrt(A.sum(axis=1))
            return d[:, None] * A * d[None, :]
        A_hat = _normalize_adj(A)
        X = H @ W + b
        out = A_hat @ X
        mean = out.mean(axis=0)
        var = out.var(axis=0)
        out = (out - mean) * jax.lax.rsqrt(var + BN_EPS) * gamma + beta
        return jax.nn.leaky_relu(out, negative_slope=LEAKY_SLOPE)
    h = jnp.maximum(_layernorm(x, axis=-1), 0.0)
    x = x + _L0_gnn_ref(h, L0_gnn_W, L0_gnn_b, L0_gnn_gamma, L0_gnn_beta, adj)
    return x

_drawn_inputs = setup_inputs


def setup_inputs(seed=0):
    import zlib

    import numpy as np

    out = dict(_drawn_inputs(seed))
    spreads = {'L0_gnn_gamma': (1.0, 0.2), 'L0_gnn_beta': (0.0, 0.1)}
    factors = {'L0_gnn_b': 22.399}
    for name, (base, spread) in spreads.items():
        noise = np.random.default_rng([zlib.crc32(name.encode()), seed]).standard_normal(out[name].shape)
        drawn = base * np.exp(spread * noise) if base else spread * noise
        out[name] = jnp.asarray(drawn.astype(out[name].dtype))
    for name, factor in factors.items():
        out[name] = (out[name] * factor).astype(out[name].dtype)
    return out
```

```python
from contextlib import ExitStack

import concourse.bass as bass
from concourse import mybir

P = 128
N = 8192
F = 64
TS = 512
G = N // TS
RB = TS // P
RING = 4
LAG = 3
KEEP_FROM = (10, 13)
CH = 8
CB = N // P // CH
LN_EPS = 1e-5
BN_EPS = 1e-5
SLOPE = 0.01


def make_schedule():
    kept = {}
    for g in range(G):
        for c in range(g + 1, G):
            if (g, c) >= KEEP_FROM:
                kept[(g, c)] = len(kept)
    steps, uses = [], []

    def use(g, c, chain, src, load):
        uses.append(dict(g=g, c=c, chain=chain, src=src, load=load, m=len(uses)))
        return uses[-1]

    loads = []
    ring_at = [0]
    arrived = {}

    def load(g, c):
        if c == g:
            target = ("diag", 0)
        elif (g, c) in kept:
            target = ("keep", kept[(g, c)])
        else:
            target = ("ring", ring_at[0] % RING)
            ring_at[0] += 1
        arrived[target] = arrived.get(target, 0) + 1
        loads.append(dict(g=g, c=c, target=target, nth=arrived[target]))
        return loads[-1]

    diag_load = {}
    keep_load = {}
    sums = {"v": 0, "a": 0}
    for g in range(G):
        pairs = min(g, G - 1 - g)
        order = []
        for i in range(pairs):
            order += [(i, "a"), (g + 1 + i, "v")]
        rest = range(2 * g + 1, G) if g < G / 2 else range(pairs, g)
        order += [(c, "va"[n % 2]) for n, c in enumerate(rest)]
        lowers = 0
        for c, by in order:
            ld = load(g, c)
            sums[by] += 1
            step = dict(kind="tile", g=g, c=c, load=ld, by=by, nth=sums[by], use=None)
            ld["sum"] = (by, sums[by])
            if (g, c) in kept:
                keep_load[(g, c)] = ld
            steps.append(step)
            if c < g:
                if lowers == min(2, g - 1):
                    dl = diag_load[g - 1]
                    dl["use"] = use(g - 1, g - 1, g - 1, ("diag", 0), dl)
                    steps.insert(-1, dict(kind="use", g=g - 1, c=g - 1, load=dl, use=dl["use"]))
                step["use"] = use(g, c, g, ld["target"], ld)
                ld["use"] = step["use"]
                lowers += 1
        ld = load(g, g)
        diag_load[g] = ld
        sums["v"] += 1
        ld["sum"] = ("v", sums["v"])
        steps.append(dict(kind="diag", g=g, c=g, load=ld, by="v", nth=sums["v"], use=None))
    chain = G
    for g in (0, 14, 1, 13, 2, 12, 3, 11, 4, 10, 5, 6, 7, 8, 9):
        for n, c in enumerate(range(g + 1, G)):
            ld = keep_load[(g, c)] if (g, c) in kept else load(g, c)
            u = use(g, c, chain, ld["target"], ld)
            ld["use"] = u
            steps.append(dict(kind="use", g=g, c=c, load=ld, use=u))
            if g == 0 and n == 1:
                dl = diag_load[G - 1]
                u = use(G - 1, G - 1, G - 1, ("diag", 0), dl)
                dl["use"] = u
                steps.append(dict(kind="use", g=G - 1, c=G - 1, load=dl, use=u))
        chain += 1
    chains = {}
    for u in uses:
        chains.setdefault(u["chain"], []).append(u)
    closes = sorted(chains.values(), key=lambda us: us[-1]["m"])
    for k, us in enumerate(closes):
        for u in us:
            u["first"] = u is us[0]
            u["last"] = u is us[-1]
            u["acc"] = u["chain"] % 2
            u["ends"] = k
    return steps, uses, loads, [us[-1] for us in closes], len(kept)


def layer_kernel(nc, x, adj, w, b, gamma, beta, consts, out):
    fp32, fp32r, bf16 = mybir.dt.float32, mybir.dt.float32r, mybir.dt.bfloat16
    ACT, ALU, AX = mybir.ActivationFunctionType, mybir.AluOpType, mybir.AxisListType
    steps, uses, loads, closing, n_keep = make_schedule()
    close_at = {}
    for k, u in enumerate(closing):
        for stage in range(1, 4):
            close_at.setdefault(u["m"] + stage, []).append((stage, k))
    n_uses = len(uses)

    adj_t = adj.rearrange("(g r p) (c k) -> g c p r k", p=P, r=RB, k=TS)
    x_t = x.rearrange("(n p) f -> p n f", p=P)
    out_t = out.rearrange("(n p) f -> p n f", p=P)
    NB = N // P

    with ExitStack() as ctx:
        def sb(name, shape, dt=fp32):
            return ctx.enter_context(nc.sbuf_tensor(name, shape, dt))

        def sem(name):
            return ctx.enter_context(nc.semaphore(name))

        ring = sb("ring", [P, RING, RB, TS])
        diag = sb("diag", [P, RB, TS])
        keep = sb("keep", [P, n_keep, RB, TS])
        y = sb("y", [P, NB, F])
        z = sb("z", [P, NB * F])
        hi = sb("hi", [P, RB, TS], fp32r)
        lo = sb("lo", [P, RB, TS], fp32r)
        ysplit = sb("ysplit", [P, 2, RB, 2 * F], fp32r)
        closed = sb("closed", [P, TS])
        cst = sb("cst", [P, 2 * P + F])
        ident, half, fold = cst[:, 0:P], cst[:, P:2 * P], cst[:, 2 * P:2 * P + F]
        w2 = sb("w2", [P, 2 * F])
        bias = sb("bias", [P, F])
        gam, bet = sb("gam", [P, 1]), sb("bet", [P, 1])
        junk = sb("junk", [P, RB, TS], bf16)
        rowsum = sb("rowsum", [P, 2, RB, G])
        deg = sb("deg", [P, G, RB])
        dinv = sb("dinv", [P, G, RB])
        power = sb("power", [P, CB])
        mean, var, rstd = sb("mean", [P, CB]), sb("var", [P, CB]), sb("rstd", [P, CB])
        xc = keep[:, n_keep - 1, 0].rearrange("p (b f) -> p b f", f=F)
        sq = keep[:, n_keep - 1, 1].rearrange("p (b f) -> p b f", f=F)
        stats = sb("stats", [P, G, 6])
        mv = sb("mv", [P, 2])
        fin = sb("fin", [P, 8])
        tail_x = keep[:, 0:2].rearrange("p a r k -> p (a r k)")
        tail_o = keep[:, 2:4].rearrange("p a r k -> p (a r k)")
        h_t = keep[:, n_keep - 1, 2]

        tp = [ctx.enter_context(nc.psum_tensor(f"tp{j}", [P, TS], fp32)) for j in range(RB)]
        acc = [ctx.enter_context(nc.psum_tensor(f"acc{j}", [P, TS], fp32)) for j in range(2)]
        m0 = ctx.enter_context(nc.psum_tensor("m0", [P, TS], fp32))
        m1 = ctx.enter_context(nc.psum_tensor("m1", [P, TS], fp32))

        def tile(target):
            kind, n = target
            return diag[:] if kind == "diag" else (ring if kind == "ring" else keep)[:, n]

        ring_in = [sem(f"ring_in{s}") for s in range(RING)]
        keep_in = [sem(f"keep_in{s}") for s in range(n_keep)]
        diag_in = sem("diag_in")
        x_in, small_in, const_in, w_in = sem("x_in"), sem("small_in"), sem("const_in"), sem("w_in")
        w_zero = sem("w_zero")
        sums_v, sums_a = sem("sums_v"), sem("sums_a")
        diag_ready = sem("diag_ready")
        tp_ready, hi_ready, lo_ready = sem("tp_ready"), sem("hi_ready"), sem("lo_ready")
        used = sem("used")
        y_hi, y_lo = sem("y_hi"), sem("y_lo")
        chain_done = sem("chain_done")
        evacuated, folded, combined = sem("evacuated"), sem("folded"), sem("combined")
        scaled, z_tp, z_stat, z_copied = sem("scaled"), sem("z_tp"), sem("z_stat"), sem("z_copied")
        deg_ready, dinv_ready, y_ready = sem("deg_ready"), sem("dinv_ready"), sem("y_ready")
        v_step, p_step = sem("v_step"), sem("p_step")
        power_set = sem("power_set")
        xc_ready, sq_ready, var_ready, rstd_ready = sem("xc_ready"), sem("sq_ready"), sem("var_ready"), sem("rstd_ready")
        h_ready, ht_tp, ht_ready, x_mm, x_ready = sem("h_ready"), sem("ht_tp"), sem("ht_ready"), sem("x_mm"), sem("x_ready")
        xl_in = sem("xl_in")
        mv_ready, mean_mm, q_ready, var_mm, bnv_ready, bnr_ready, ab_ready = (
            sem(n) for n in ("mv_ready", "mean_mm", "q_ready", "var_mm", "bnv_ready", "bnr_ready", "ab_ready"))
        affine, act_done, out_tp, out_ready, out_st = sem("affine"), sem("act_done"), sem("out_tp"), sem("out_ready"), sem("out_st")

        def wait_load(eng, ld):
            kind, n = ld["target"]
            eng.wait_ge(diag_in if kind == "diag" else (ring_in if kind == "ring" else keep_in)[n], 16 * ld["nth"])

        def prologue(n, stage):
            return n // 4 if n < 4 * CH and n % 4 == stage else None

        block = ctx.enter_context(nc.Block())

        @block.sync
        def _(sp):
            sp.dma_start(z[:], x_t).then_inc(x_in, 16)
            last = {}
            for ld in loads:
                before = last.get(ld["target"])
                if before is not None:
                    if "sum" in before and before["target"][0] != "diag":
                        sp.wait_ge(sums_v if before["sum"][0] == "v" else sums_a, before["sum"][1])
                    if "use" in before:
                        sp.wait_ge(tp_ready, RB * (before["use"]["m"] + 1))
                kind, n = ld["target"]
                s = diag_in if kind == "diag" else (ring_in if kind == "ring" else keep_in)[n]
                sp.dma_start(tile(ld["target"]), adj_t[ld["g"], ld["c"]]).then_inc(s, 16)
                last[ld["target"]] = ld
            sp.wait_ge(tp_ready, RB * (1 + max(u["m"] for u in uses if u["src"][0] == "keep")))
            sp.dma_start(tail_x, x_t).then_inc(xl_in, 16)
            for t in range(CH):
                sp.wait_ge(out_ready, t + 1)
                sp.dma_start(out_t[:, CB * t:CB * (t + 1), :],
                             tail_o[:, CB * F * t:CB * F * (t + 1)]).then_inc(out_st, 16)
            sp.wait_ge(out_st, 16 * CH)

        @block.gpsimd
        def _(pool):
            nc.gpsimd.memset(power[:], -0.5).then_inc(power_set, 1)
            pool.wait_ge(power_set, 1)
            seen_groups = [0]

            def scale_group(g):
                pool.wait_ge(deg_ready, g + 1)
                nc.gpsimd.tensor_tensor(dinv[:, g], deg[:, g], power[:, 0:RB], ALU.pow).then_inc(dinv_ready, 1)
                pool.wait_ge(dinv_ready, g + 1)
                pool.wait_ge(x_ready, g // 2 + 1)
                rows = y[:, RB * g:RB * (g + 1), :]
                nc.gpsimd.tensor_tensor(rows, rows, dinv[:, g].unsqueeze(2).to_broadcast([P, RB, F]),
                                        ALU.mult).then_inc(y_ready, 1)
                pool.wait_ge(y_ready, g + 1)

            for n, step in enumerate(steps):
                u = step["use"]
                if u is not None:
                    m, c = u["m"], u["c"]
                    if c == u["g"]:
                        scale_group(c)
                    if m >= 2:
                        pool.wait_ge(used, RB * (m - 1))
                    rows = y[:, RB * c:RB * (c + 1), :]
                    s = ysplit[:, m % 2]
                    nc.gpsimd.tensor_copy(s[:, :, 0:F], rows).then_inc(y_hi, 1)
                    pool.wait_ge(y_hi, m + 1)
                    nc.gpsimd.tensor_tensor(s[:, :, F:2 * F], rows, s[:, :, 0:F].bitcast(fp32),
                                            ALU.subtract).then_inc(y_lo, 1)
                t = prologue(n, 1)
                if t is not None:
                    pool.wait_ge(var_ready, t + 1)
                    nc.gpsimd.tensor_tensor(rstd[:], var[:], power[:], ALU.pow).then_inc(rstd_ready, 1)
            pool.wait_ge(bnv_ready, 1)
            nc.gpsimd.tensor_tensor(fin[:, 3:4], fin[:, 2:3], power[:, 0:1], ALU.pow).then_inc(bnr_ready, 1)

        @block.tensor
        def _(pe):
            def transposes(u, j):
                m = u["m"]
                if j == 0:
                    if u["src"][0] == "diag":
                        pe.wait_ge(diag_ready, u["g"] + 1)
                    else:
                        wait_load(pe, u["load"])
                if m >= 1:
                    pe.wait_ge(lo_ready, RB * (m - 1) + j + 1)
                for r in range(RB):
                    last = nc.tensor.transpose(tp[j][:, P * r:P * (r + 1)],
                                               tile(u["src"])[:, r, P * j:P * (j + 1)], ident)
                last.then_inc(tp_ready, 1)

            def products(u, j):
                m = u["m"]
                if j == 0:
                    pe.wait_ge(y_lo, m + 1)
                    if u["first"] and u["chain"] >= 2:
                        pe.wait_ge(evacuated, [v["chain"] for v in closing].index(u["chain"] - 2) + 1)
                pe.wait_ge(hi_ready, RB * m + j + 1)
                nc.tensor.matmul(acc[u["acc"]][:], ysplit[:, m % 2, j, :], hi[:, j, :],
                                 start=u["first"] and j == 0, stop=False)
                pe.wait_ge(lo_ready, RB * m + j + 1)
                nc.tensor.matmul(acc[u["acc"]][:], ysplit[:, m % 2, j, :], lo[:, j, :],
                                 start=False, stop=u["last"] and j == RB - 1).then_inc(used, 1)

            def close(stage, k):
                if stage == 2:
                    pe.wait_ge(evacuated, k + 1)
                    if k >= 1:
                        pe.wait_ge(combined, k)
                    else:
                        pe.wait_ge(ht_ready, CH)
                    for r in range(RB):
                        last = nc.tensor.matmul(m0[:, F * r:F * (r + 1)], closed[:, P * r:P * (r + 1)], fold,
                                                start=True, stop=True)
                    last.then_inc(folded, 1)
                if stage == 3 and k >= G - 1:
                    f = k - (G - 1)
                    pe.wait_ge(scaled, f + 1)
                    if f >= 1:
                        pe.wait_ge(z_copied, f)
                    g = closing[k]["g"]
                    for r in range(2):
                        last = nc.tensor.transpose(m1[:, P * r:P * (r + 1)],
                                                   z[:, 2 * P * g + P * r:2 * P * g + P * (r + 1)], ident)
                    last.then_inc(z_tp, 1)

            pe.wait_ge(const_in, 16)
            u_done = 0
            for n, step in enumerate(steps):
                t = prologue(n, 2)
                if t is not None:
                    pe.wait_ge(h_ready, t + 1)
                    for r in range(RB):
                        last = nc.tensor.transpose(m0[:, P * r:P * (r + 1)],
                                                   xc[:, 2 * r:2 * r + 2, :].rearrange("p b f -> p (b f)"), ident)
                    last.then_inc(ht_tp, 1)
                t = prologue(n, 3)
                if t is not None:
                    if t == 0:
                        pe.wait_ge(w_in, 32)
                    pe.wait_ge(ht_ready, t + 1)
                    if t >= 1:
                        pe.wait_ge(x_ready, t)
                    for r in range(RB):
                        last = nc.tensor.matmul(m1[:, P * r:P * (r + 1)], h_t[:, P * r:P * (r + 1)], w2[:],
                                                start=True, stop=True)
                    last.then_inc(x_mm, 1)
                u = step["use"]
                if u is None:
                    continue
                for j in range(RB):
                    transposes(u, j)
                    v = RB * u["m"] + j - LAG
                    if v >= 0:
                        products(uses[v // RB], v % RB)
                for stage, k in close_at.get(u["m"], ()):
                    close(stage, k)
            for v in range(RB * n_uses - LAG, RB * n_uses):
                products(uses[v // RB], v % RB)
            for m in range(n_uses, n_uses + 3):
                for stage, k in close_at.get(m, ()):
                    close(stage, k)
            pe.wait_ge(mv_ready, 1)
            pe.wait_ge(z_copied, G)
            nc.tensor.matmul(m1[:, 0:1], half, mv[:, 0:1], start=True, stop=True).then_inc(mean_mm, 1)
            pe.wait_ge(q_ready, 1)
            nc.tensor.matmul(m0[:, 0:1], half, fin[:, 1:2], start=True, stop=True).then_inc(var_mm, 1)
            for t in range(CH):
                pe.wait_ge(act_done, t + 1)
                if t >= RB:
                    pe.wait_ge(out_ready, t - RB + 1)
                for r in range(RB):
                    at = CB * F * t + P * r
                    last = nc.tensor.transpose(tp[t % RB][:, P * r:P * (r + 1)], z[:, at:at + P], ident)
                last.then_inc(out_tp, 1)

        @block.scalar
        def _(act):
            act.dma_start(cst[:], consts).then_inc(const_in, 16)
            act.wait_ge(w_zero, 1)
            act.dma_start(w2[0:F, 0:F], w).then_inc(w_in, 16)
            act.dma_start(w2[F:P, F:P], w).then_inc(w_in, 16)
            act.dma_start(bias[:], b.unsqueeze(0).to_broadcast([P, F])).then_inc(small_in, 16)
            for s, v in ((gam, gamma), (bet, beta)):
                for half_at in (0, F):
                    act.dma_start(s[half_at:half_at + F, :], v.unsqueeze(1)).then_inc(small_in, 16)

            def close(stage, k):
                if stage == 1:
                    act.wait_ge(chain_done_value(k)[0], chain_done_value(k)[1])
                    if k >= 1:
                        act.wait_ge(folded, k)
                    nc.scalar.activation(closed[:], acc[closing[k]["acc"]][:], ACT.Copy).then_inc(evacuated, 1)
                if stage == 3 and k >= G - 1:
                    f = k - (G - 1)
                    g = closing[k]["g"]
                    act.wait_ge(z_stat, f + 1)
                    nc.scalar.activation(z[:, 2 * P * g:2 * P * (g + 1)], m1[:, 0:2 * P],
                                         ACT.Copy).then_inc(z_copied, 1)

            def chain_done_value(k):
                return used, RB * (closing[k]["m"] + 1)

            for n, step in enumerate(steps):
                u = step["use"]
                if u is not None:
                    m = u["m"]
                    for j in range(RB):
                        act.wait_ge(tp_ready, RB * m + j + 1)
                        if m >= 1:
                            act.wait_ge(used, RB * (m - 1) + j + 1)
                        nc.scalar.activation(hi[:, j, :], tp[j][:], ACT.Copy).then_inc(hi_ready, 1)
                if step["kind"] == "tile" and step["by"] == "a":
                    wait_load(act, step["load"])
                    g, c = step["g"], step["c"]
                    if g >= 2:
                        act.wait_ge(deg_ready, g - 1)
                    if step["nth"] > 1:
                        act.wait_ge(sums_a, step["nth"] - 1)
                    for r in range(RB):
                        last = nc.scalar.activation(junk[:, r, :], tile(step["load"]["target"])[:, r, :], ACT.Copy,
                                                    accum_out=rowsum[:, g % 2, r, c:c + 1])
                    last.then_inc(sums_a, 1)
                t = prologue(n, 0)
                if t is not None:
                    act.wait_ge(xc_ready, t + 1)
                    nc.scalar.activation(sq, xc, ACT.Square).then_inc(sq_ready, 1)
                t = prologue(n, 2)
                if t is not None:
                    act.wait_ge(ht_tp, t + 1)
                    if t >= 1:
                        act.wait_ge(x_mm, t)
                    nc.scalar.activation(h_t, m0[:], ACT.Copy).then_inc(ht_ready, 1)
                if u is not None:
                    for stage, k in close_at.get(u["m"], ()):
                        close(stage, k)
            for m in range(n_uses, n_uses + 3):
                for stage, k in close_at.get(m, ()):
                    close(stage, k)
            act.wait_ge(ab_ready, 1)
            for t in range(CH):
                part = z[:, CB * F * t:CB * F * (t + 1)]
                nc.scalar.activation(part, part, ACT.Identity, bias=fin[:, 6:7],
                                     scale=fin[:, 5:6]).then_inc(affine, 1)

        @block.vector
        def _(dve):
            nc.vector.memset(w2[:], 0.0).then_inc(w_zero, 1)
            own = [0]

            def link(ins):
                own[0] += 1
                ins.then_inc(v_step, 1)
                dve.wait_ge(v_step, own[0])

            def close(stage, k):
                g = closing[k]["g"]
                zg = z[:, 2 * P * g:2 * P * (g + 1)]
                if stage == 2:
                    dve.wait_ge(folded, k + 1)
                    if k < G - 1:
                        nc.vector.tensor_copy(zg, m0[:, 0:2 * P]).then_inc(combined, 1)
                    else:
                        f = k - (G - 1)
                        rows = zg.rearrange("p (r f) -> p r f", f=F)
                        new = m0[:, 0:2 * P].rearrange("p (r f) -> p r f", f=F)
                        by = dinv[:, g].unsqueeze(2).to_broadcast([P, RB, F])
                        if k > G - 1:
                            nc.vector.tensor_tensor(rows, new, rows, ALU.add).then_inc(combined, 1)
                            dve.wait_ge(combined, k + 1)
                            nc.vector.tensor_tensor(rows, rows, by, ALU.mult).then_inc(scaled, 1)
                        else:
                            dve.wait_ge(dinv_ready, G)
                            link(nc.vector.tensor_tensor(rows, new, by, ALU.mult))
                            dve.sem_inc(combined, 1)
                            dve.sem_inc(scaled, 1)
                if stage == 3 and k >= G - 1:
                    f = k - (G - 1)
                    dve.wait_ge(z_tp, f + 1)
                    nc.vector.bn_stats(stats[:, f, :], m1[:, 0:2 * P]).then_inc(z_stat, 1)

            for n, step in enumerate(steps):
                u = step["use"]
                if u is not None:
                    m = u["m"]
                    for j in range(RB):
                        dve.wait_ge(hi_ready, RB * m + j + 1)
                        if m >= 1:
                            dve.wait_ge(used, RB * (m - 1) + j + 1)
                        nc.vector.tensor_tensor(lo[:, j, :], tp[j][:], hi[:, j, :].bitcast(fp32),
                                                ALU.subtract).then_inc(lo_ready, 1)
                g, c = step["g"], step["c"]
                if step["kind"] == "tile" and step["by"] == "v":
                    wait_load(dve, step["load"])
                    nc.vector.tensor_reduce(rowsum[:, g % 2, :, c:c + 1], tile(step["load"]["target"]),
                                            AX.X, ALU.add).then_inc(sums_v, 1)
                if step["kind"] == "diag":
                    wait_load(dve, step["load"])
                    for r in range(RB):
                        at = diag[:, r, P * r:P * (r + 1)]
                        last = nc.vector.tensor_tensor(at, at, ident, ALU.add)
                    last.then_inc(diag_ready, 1)
                    dve.wait_ge(diag_ready, g + 1)
                    nc.vector.tensor_reduce(rowsum[:, g % 2, :, c:c + 1], diag[:], AX.X, ALU.add).then_inc(sums_v, 1)
                    dve.wait_ge(sums_v, step["nth"])
                    dve.wait_ge(sums_a, max(s["nth"] for s in steps[:n] if s["kind"] == "tile" and s["by"] == "a"))
                    nc.vector.tensor_reduce(deg[:, g].unsqueeze(2), rowsum[:, g % 2], AX.X, ALU.add).then_inc(deg_ready, 1)
                t = prologue(n, 0)
                if t is not None:
                    xs = z[:, CB * F * t:CB * F * (t + 1)].rearrange("p (b f) -> p b f", f=F)
                    if t == 0:
                        dve.wait_ge(x_in, 16)
                        dve.wait_ge(const_in, 16)
                        dve.wait_ge(small_in, 80)
                    else:
                        dve.wait_ge(ht_tp, t)
                    link(nc.vector.tensor_reduce(mean[:].unsqueeze(2), xs, AX.X, ALU.add))
                    link(nc.vector.tensor_scalar(mean[:], mean[:], 1.0 / F, None, ALU.mult))
                    nc.vector.tensor_tensor(xc, xs, mean[:].unsqueeze(2).to_broadcast([P, CB, F]),
                                            ALU.subtract).then_inc(xc_ready, 1)
                t = prologue(n, 1)
                if t is not None:
                    dve.wait_ge(sq_ready, t + 1)
                    link(nc.vector.tensor_reduce(var[:].unsqueeze(2), sq, AX.X, ALU.add))
                    nc.vector.tensor_scalar(var[:], var[:], 1.0 / F, LN_EPS, ALU.mult, ALU.add).then_inc(var_ready, 1)
                t = prologue(n, 2)
                if t is not None:
                    dve.wait_ge(rstd_ready, t + 1)
                    link(nc.vector.tensor_scalar(xc, xc, 0.0, None, ALU.max))
                    nc.vector.tensor_tensor(xc, xc, rstd[:].unsqueeze(2).to_broadcast([P, CB, F]),
                                            ALU.mult).then_inc(h_ready, 1)
                t = prologue(n, 3)
                if t is not None:
                    dve.wait_ge(x_mm, t + 1)
                    nc.vector.tensor_tensor(y[:, CB * t:CB * (t + 1), :],
                                            m1[:].rearrange("p (b f) -> p b f", f=F),
                                            bias[:].unsqueeze(1).to_broadcast([P, CB, F]), ALU.add).then_inc(x_ready, 1)
                if u is not None:
                    for stage, k in close_at.get(u["m"], ()):
                        close(stage, k)
            for m in range(n_uses, n_uses + 3):
                for stage, k in close_at.get(m, ()):
                    close(stage, k)
            dve.wait_ge(z_stat, G)
            nc.vector.bn_aggr(mv[:], stats[:].rearrange("p g s -> p (g s)")).then_inc(mv_ready, 1)
            dve.wait_ge(mean_mm, 1)
            dve.wait_ge(mv_ready, 1)
            link(nc.vector.tensor_copy(fin[:, 4:5], m1[:, 0:1]))
            link(nc.vector.tensor_tensor(fin[:, 0:1], mv[:, 0:1], fin[:, 4:5], ALU.subtract))
            link(nc.vector.tensor_tensor(fin[:, 1:2], fin[:, 0:1], fin[:, 0:1], ALU.mult))
            nc.vector.tensor_tensor(fin[:, 1:2], fin[:, 1:2], mv[:, 1:2], ALU.add).then_inc(q_ready, 1)
            dve.wait_ge(var_mm, 1)
            nc.vector.tensor_scalar(fin[:, 2:3], m0[:, 0:1], BN_EPS, None, ALU.add).then_inc(bnv_ready, 1)
            dve.wait_ge(bnr_ready, 1)
            link(nc.vector.tensor_tensor(fin[:, 5:6], fin[:, 3:4], gam[:], ALU.mult))
            link(nc.vector.tensor_tensor(fin[:, 7:8], fin[:, 4:5], fin[:, 5:6], ALU.mult))
            nc.vector.tensor_tensor(fin[:, 6:7], bet[:], fin[:, 7:8], ALU.subtract).then_inc(ab_ready, 1)

            def leaky(t):
                dve.wait_ge(affine, t + 1)
                part = z[:, CB * F * t:CB * F * (t + 1)]
                nc.vector.scalar_tensor_tensor(part, part, SLOPE, part, ALU.mult, ALU.max).then_inc(act_done, 1)

            leaky(0)
            dve.wait_ge(xl_in, 16)
            for t in range(CH):
                if t + 1 < CH:
                    leaky(t + 1)
                dve.wait_ge(out_tp, t + 1)
                span = slice(CB * F * t, CB * F * (t + 1))
                nc.vector.tensor_tensor(tail_o[:, span], tp[t % RB][:], tail_x[:, span],
                                        ALU.add).then_inc(out_ready, 1)


def kernel(x, adj, L0_gnn_W, L0_gnn_b, L0_gnn_gamma, L0_gnn_beta):
    import numpy as np
    import concourse.bacc as bacc
    from concourse.bass_utils import run_bass_kernel_spmd

    eye = np.eye(P, dtype=np.float32)
    same = np.tile(np.eye(F, dtype=np.float32), (2, 1))
    consts = np.concatenate([eye, 0.5 * np.tile(same, (1, 2)), same], axis=1)
    arrays = {"x": x, "adj": adj, "w": L0_gnn_W, "b": L0_gnn_b, "gamma": L0_gnn_gamma, "beta": L0_gnn_beta,
              "consts": consts}
    arrays = {f"{k}_dram": np.ascontiguousarray(v) for k, v in arrays.items()}
    nc = bacc.Bacc("TRN2", target_bir_lowering=False, num_devices=1)
    args = [nc.dram_tensor(k, v.shape, mybir.dt.from_np(v.dtype), kind="ExternalInput").ap()
            for k, v in arrays.items()]
    out = nc.dram_tensor("out_dram", (N, F), mybir.dt.float32, kind="ExternalOutput").ap()
    layer_kernel(nc, *args, out)
    return run_bass_kernel_spmd(nc, [arrays], core_ids=[0]).results[0]["out_dram"]
```

```python
from contextlib import ExitStack

import concourse.bass as bass
from concourse import mybir

P = 128
N = 8192
F = 64
TS = 512
G = N // TS
RB = TS // P
RING = 5
DEPTH = 5
LAG = DEPTH - 1
BAND = 3
N_KEEP = (BAND + 1) * BAND
EARLY = {8: (0,), 9: (1, 2), 10: (3,)}
EARLY_TO = 8
LAST_ROWS = (0, 12, 1, 13, 2, 14, 3, 4, 5, 6, 7, 8, 9, 10, 11)
CH = G // 2
CB = N // P // CH
LN_EPS = 1e-5
BN_EPS = 1e-5
SLOPE = 0.01


def make_schedule():
    steps, uses, loads, chains = [], [], [], []
    count = dict(ring=0, v=0, a=0)
    arrived = {}
    kept = {}
    busy = dict(v=0.0, a=0.0)

    def load(g, c, again=False):
        if c == g:
            place = ("diag", 0)
        elif not again and 0 < c - g <= BAND:
            place = ("keep", (g % (BAND + 1)) * BAND + c - g - 1)
        else:
            place = ("ring", count["ring"] % RING)
            count["ring"] += 1
        arrived[place] = arrived.get(place, 0) + 1
        loads.append(dict(g=g, c=c, place=place, nth=arrived[place], sum=None, use=None))
        if place[0] != "ring":
            kept[(g, c)] = loads[-1]
        return loads[-1]

    def new_chain(acc):
        chains.append(dict(acc=acc, uses=[]))
        return chains[-1]

    def add_use(ld, chain):
        u = dict(g=ld["g"], c=ld["c"], chain=chain, load=ld, m=len(uses))
        uses.append(u)
        chain["uses"].append(u)
        ld["use"] = u
        busy["v"] += 2.4
        busy["a"] += 1.9
        return u

    def summed(ld):
        for e in busy:
            busy[e] *= 0.9
        by = "v" if ld["c"] == ld["g"] or busy["v"] + 2.2 <= busy["a"] + 2.45 else "a"
        busy[by] += 2.2 if by == "v" else 2.45
        count[by] += 1
        ld["sum"] = (by, count[by])

    row_chain = {}
    for g in range(G):
        row_chain[g] = new_chain(g % 2)
        lower, upper = list(range(g)), list(range(g + 1 + BAND, G)) + list(range(g + 1, min(g + 1 + BAND, G)))
        order = []
        while lower or upper:
            if len(lower) * (G - 1 - g) >= len(upper) * g and lower:
                order.append(lower.pop(0))
            else:
                order.append(upper.pop(0))
        extra = []
        if g >= 1:
            extra.append((g - 1, g - 1, False, row_chain[g - 1]))
        if g >= BAND + 1:
            chain = new_chain((g - 1) % 2)
            r = g - 1 - BAND
            extra += [(r, c, False, chain) for c in range(r + 1, r + 1 + BAND)]
        for r in EARLY.get(g, ()):
            chain = new_chain((g - 1) % 2)
            extra += [(r, c, True, chain) for c in range(r + 1 + BAND, EARLY_TO)]
        first = min(2, g - 1)
        gap = max(1, (G - 1 - BAND - first) // (len(extra) + 1))
        lowers = since = 0

        def do_extra():
            r, c, again, chain = extra.pop(0)
            ld = load(r, c, True) if again else kept[(r, c)]
            steps.append(dict(kind="use", g=r, c=c, load=ld, use=add_use(ld, chain)))

        for c in order:
            started = lowers > first or (lowers == first and c < g)
            if extra and started and (since % gap == 0 or c == g - 1 and extra[0][0:2] == (g - 1, g - 1)):
                do_extra()
            since += started
            while 0 < c - g <= BAND and any(r == g - 1 - BAND for r, *_ in extra):
                do_extra()
            ld = load(g, c)
            u = None
            if c < g:
                u = add_use(ld, row_chain[g])
                lowers += 1
            summed(ld)
            steps.append(dict(kind="tile", g=g, c=c, load=ld, use=u))
        while extra:
            do_extra()
        ld = load(g, g)
        summed(ld)
        steps.append(dict(kind="diag", g=g, c=g, load=ld, use=None, sums_a=count["a"]))
    for step, then in zip(steps, steps[1:] + [None]):
        own = [step["load"]] if step["kind"] == "tile" else []
        step["sums"] = step.get("sums", []) + own
        if own and step["use"] is None and then and then["use"]:
            step["sums"], then["sums"] = [], step["sums"]
    acc = 0
    for n, g in enumerate(LAST_ROWS):
        chain = new_chain(acc)
        acc = 1 - acc
        start = (EARLY_TO if g < EARLY_TO - BAND - 1 else g + 1 + BAND) if g < G - 1 - BAND else g + 1
        for i, c in enumerate(range(start, G)):
            if n == 0 and i == 2:
                ld = kept[(G - 1, G - 1)]
                steps.append(dict(kind="use", g=G - 1, c=G - 1, load=ld, sums=[], use=add_use(ld, row_chain[G - 1])))
            ld = kept[(g, c)] if c - g <= BAND else load(g, c, True)
            steps.append(dict(kind="use", g=g, c=c, load=ld, sums=[], use=add_use(ld, chain)))
    chains.sort(key=lambda ch: ch["uses"][-1]["m"])
    rows = [ch["uses"][0]["g"] for ch in chains]
    finals, closed_rows, pairs = 0, set(), 0
    for k, ch in enumerate(chains):
        ch["k"], ch["g"] = k, rows[k]
        ch["opens"] = rows[k] not in rows[:k]
        ch["final"] = finals if rows[k] not in rows[k + 1:] else None
        finals += ch["final"] is not None
        if ch["final"] is not None:
            closed_rows.add(rows[k])
        ch["pair"] = pairs if ch["final"] is not None and rows[k] ^ 1 in closed_rows else None
        pairs += ch["pair"] is not None
        begins = ch["uses"][0]["m"]
        before = [o["k"] for o in chains[:k] if o["acc"] == ch["acc"]]
        assert all(chains[o]["uses"][-1]["m"] < begins for o in before)
        ch["after"] = max(before, default=None)
    assert finals == G and len(uses) == G * G
    return steps, uses, loads, chains


def layer_kernel(nc, x, adj, w, b, gamma, beta, consts, out):
    fp32, fp32r = mybir.dt.float32, mybir.dt.float32r
    ACT, ALU, AX = mybir.ActivationFunctionType, mybir.AluOpType, mybir.AxisListType
    steps, uses, loads, chains = make_schedule()
    close_at = {}
    for ch in chains:
        for stage in range(1, 4):
            close_at.setdefault(ch["uses"][-1]["m"] + stage, []).append((stage, ch))
    n_uses = len(uses)

    adj_t = adj.rearrange("(g r p) (c k) -> g c p r k", p=P, r=RB, k=TS)
    x_t = x.rearrange("(n p i) f -> p n (i f)", p=P, i=RB)
    out_t = out.rearrange("(t h p i) f -> p t h (i f)", h=2, p=P, i=RB)
    NB = N // P

    with ExitStack() as ctx:
        def sb(name, shape, dt=fp32):
            return ctx.enter_context(nc.sbuf_tensor(name, shape, dt))

        def sem(name):
            return ctx.enter_context(nc.semaphore(name))

        ring = sb("ring", [P, RING, RB, TS])
        diag = sb("diag", [P, RB, TS])
        keep = sb("keep", [P, N_KEEP, RB, TS])
        y = sb("y", [P, NB, F])
        z = sb("z", [P, NB * F])
        hi = sb("hi", [P, DEPTH, TS], fp32r)
        lo = sb("lo", [P, DEPTH, TS], fp32r)
        ysplit = sb("ysplit", [P, 2, RB, 2 * F], fp32r)
        closed = sb("closed", [P, TS])
        cst = sb("cst", [P, 2 * P + F])
        ident, half, fold = cst[:, 0:P], cst[:, P:2 * P], cst[:, 2 * P:2 * P + F]
        w2 = sb("w2", [P, 2 * F])
        bias = sb("bias", [P, F])
        gam, bet = sb("gam", [P, 1]), sb("bet", [P, 1])
        junk = sb("junk", [P, 2, TS], mybir.dt.bfloat16)
        rowsum = sb("rowsum", [P, 2, RB, G])
        deg = sb("deg", [P, G, RB])
        dinv = sb("dinv", [P, G, RB])
        power = sb("power", [P, CB])
        mean, var, rstd = sb("mean", [P, CB]), sb("var", [P, CB]), sb("rstd", [P, CB])
        xc = keep[:, N_KEEP - 1, 0].rearrange("p (b f) -> p b f", f=F)
        sq = keep[:, N_KEEP - 1, 1].rearrange("p (b f) -> p b f", f=F)
        stats = sb("stats", [P, CH, 6])
        mv = sb("mv", [P, 2])
        fin = sb("fin", [P, 8])
        tail_x = keep[:, 0:2].rearrange("p a r k -> p (a r k)").rearrange("p (t h k) -> p t h k", t=CH, h=2)
        tail_o = keep[:, 2:4].rearrange("p a r k -> p (a r k)").rearrange("p (t h k) -> p t h k", t=CH, h=2)
        h_t = keep[:, N_KEEP - 1, 2]

        tp = [ctx.enter_context(nc.psum_tensor(f"tp{j}", [P, TS], fp32)) for j in range(DEPTH)]
        acc = [ctx.enter_context(nc.psum_tensor(f"acc{j}", [P, TS], fp32)) for j in range(2)]
        m0 = ctx.enter_context(nc.psum_tensor("m0", [P, TS], fp32))

        def z_pair(g):
            return z[:, 4 * P * (g // 2):4 * P * (g // 2 + 1)]

        def tile(place):
            kind, n = place
            return diag[:] if kind == "diag" else (ring if kind == "ring" else keep)[:, n]

        ring_in = [sem(f"ring_in{s}") for s in range(RING)]
        keep_in = [sem(f"keep_in{s}") for s in range(N_KEEP)]
        diag_in = sem("diag_in")
        x_in, small_in, const_in, w_in = sem("x_in"), sem("small_in"), sem("const_in"), sem("w_in")
        w_zero = sem("w_zero")
        sums_v, sums_a = sem("sums_v"), sem("sums_a")
        diag_ready = sem("diag_ready")
        tp_ready, hi_ready, lo_ready = sem("tp_ready"), sem("hi_ready"), sem("lo_ready")
        used = sem("used")
        y_hi, y_lo = sem("y_hi"), sem("y_lo")
        chain_done = sem("chain_done")
        evacuated, folded, combined = sem("evacuated"), sem("folded"), sem("combined")
        scaled, z_tp, z_stat, z_copied = sem("scaled"), sem("z_tp"), sem("z_stat"), sem("z_copied")
        deg_ready, dinv_ready, y_ready = sem("deg_ready"), sem("dinv_ready"), sem("y_ready")
        v_step, p_step = sem("v_step"), sem("p_step")
        power_set = sem("power_set")
        xc_ready, sq_ready, var_ready, rstd_ready = sem("xc_ready"), sem("sq_ready"), sem("var_ready"), sem("rstd_ready")
        h_ready, ht_tp, ht_ready, x_mm, x_ready = sem("h_ready"), sem("ht_tp"), sem("ht_ready"), sem("x_mm"), sem("x_ready")
        xl_in = sem("xl_in")
        mv_ready, mean_mm, q_ready, var_mm, bnv_ready, bnr_ready, ab_ready = (
            sem(n) for n in ("mv_ready", "mean_mm", "q_ready", "var_mm", "bnv_ready", "bnr_ready", "ab_ready"))
        affine, act_done, out_tp, out_ready, out_st = sem("affine"), sem("act_done"), sem("out_tp"), sem("out_ready"), sem("out_st")

        def wait_load(eng, ld):
            kind, n = ld["place"]
            eng.wait_ge(diag_in if kind == "diag" else (ring_in if kind == "ring" else keep_in)[n], 16 * ld["nth"])

        def in_turn(step, by, part_of_use, part_of_sum):
            parts = [(ld, r) for ld in step["sums"] if ld["sum"][0] == by for r in range(RB)]
            slots = RB if step["use"] else 1
            for j in range(slots):
                for ld, r in parts[len(parts) * j // slots:len(parts) * (j + 1) // slots]:
                    part_of_sum(ld, r)
                if step["use"]:
                    part_of_use(step["use"]["m"], j)

        def prologue(n, stage):
            n -= stage
            return n // 4 if 0 <= n < 4 * CH and n % 4 == 0 else None

        block = ctx.enter_context(nc.Block())

        @block.sync
        def _(sp):
            sp.dma_start(z[:].rearrange("p (n k) -> p n k", n=G), x_t).then_inc(x_in, 16)
            last = {}
            for ld in loads:
                before = last.get(ld["place"])
                if before is not None:
                    if before["sum"]:
                        by, nth = before["sum"]
                        sp.wait_ge(sums_v if by == "v" else sums_a, nth if by == "v" else RB * nth)
                    if before["use"]:
                        sp.wait_ge(tp_ready, RB * (before["use"]["m"] + 1))
                kind, n = ld["place"]
                s = diag_in if kind == "diag" else (ring_in if kind == "ring" else keep_in)[n]
                sp.dma_start(tile(ld["place"]), adj_t[ld["g"], ld["c"]]).then_inc(s, 16)
                last[ld["place"]] = ld
            sp.wait_ge(tp_ready, RB * (1 + max(u["m"] for u in uses if u["load"]["place"][0] == "keep")))
            sp.dma_start(tail_x.rearrange("p t h k -> p (t h) k"), x_t).then_inc(xl_in, 16)
            for t in range(CH):
                sp.wait_ge(out_ready, t + 1)
                sp.dma_start(out_t[:, t], tail_o[:, t]).then_inc(out_st, 16)
            sp.wait_ge(out_st, 16 * CH)

        @block.gpsimd
        def _(pool):
            nc.gpsimd.memset(power[:], -0.5).then_inc(power_set, 1)
            pool.wait_ge(power_set, 1)

            def scale_group(g):
                pool.wait_ge(deg_ready, g + 1)
                nc.gpsimd.tensor_tensor(dinv[:, g], deg[:, g], power[:, 0:RB], ALU.pow).then_inc(dinv_ready, 1)
                pool.wait_ge(dinv_ready, g + 1)
                pool.wait_ge(x_ready, g // 2 + 1)
                rows = y[:, RB * g:RB * (g + 1), :]
                nc.gpsimd.tensor_tensor(rows, rows, dinv[:, g].unsqueeze(2).to_broadcast([P, RB, F]),
                                        ALU.mult).then_inc(y_ready, 1)
                pool.wait_ge(y_ready, g + 1)

            for n, step in enumerate(steps):
                u = step["use"]
                if u is not None:
                    m, c = u["m"], u["c"]
                    if c == u["g"]:
                        scale_group(c)
                    if m >= 2:
                        pool.wait_ge(used, RB * (m - 1))
                    rows = y[:, RB * c:RB * (c + 1), :]
                    s = ysplit[:, m % 2]
                    nc.gpsimd.tensor_copy(s[:, :, 0:F], rows).then_inc(y_hi, 1)
                    pool.wait_ge(y_hi, m + 1)
                    nc.gpsimd.tensor_tensor(s[:, :, F:2 * F], rows, s[:, :, 0:F].bitcast(fp32),
                                            ALU.subtract).then_inc(y_lo, 1)
                t = prologue(n, 1)
                if t is not None:
                    pool.wait_ge(var_ready, t + 1)
                    nc.gpsimd.tensor_tensor(rstd[:], var[:], power[:], ALU.pow).then_inc(rstd_ready, 1)
            pool.wait_ge(bnv_ready, 1)
            nc.gpsimd.tensor_tensor(fin[:, 3:4], fin[:, 2:3], power[:, 0:1], ALU.pow).then_inc(bnr_ready, 1)

        @block.tensor
        def _(pe):
            def transposes(u, j):
                v = RB * u["m"] + j
                if j == 0:
                    if u["load"]["place"][0] == "diag":
                        pe.wait_ge(diag_ready, u["g"] + 1)
                    else:
                        wait_load(pe, u["load"])
                if v >= DEPTH:
                    pe.wait_ge(lo_ready, v - DEPTH + 1)
                for r in range(RB):
                    last = nc.tensor.transpose(tp[v % DEPTH][:, P * r:P * (r + 1)],
                                               tile(u["load"]["place"])[:, r, P * j:P * (j + 1)], ident)
                last.then_inc(tp_ready, 1)

            def products(u, j):
                m, ch = u["m"], u["chain"]
                first, last = u is ch["uses"][0], u is ch["uses"][-1]
                bank = acc[ch["acc"]][:]
                v = RB * m + j
                if j == 0:
                    pe.wait_ge(y_lo, m + 1)
                    if first and ch["after"] is not None:
                        pe.wait_ge(evacuated, ch["after"] + 1)
                pe.wait_ge(hi_ready, v + 1)
                nc.tensor.matmul(bank, ysplit[:, m % 2, j, :], hi[:, v % DEPTH, :],
                                 start=first and j == 0, stop=False)
                pe.wait_ge(lo_ready, v + 1)
                nc.tensor.matmul(bank, ysplit[:, m % 2, j, :], lo[:, v % DEPTH, :],
                                 start=False, stop=last and j == RB - 1).then_inc(used, 1)

            def close(stage, ch):
                k, g, f = ch["k"], ch["g"], ch["final"]
                if stage == 2:
                    pe.wait_ge(evacuated, k + 1)
                    if k >= 1:
                        pe.wait_ge(combined, k)
                        if before := [o["pair"] for o in chains[:k] if o["pair"] is not None]:
                            pe.wait_ge(z_copied, before[-1] + 1)
                    else:
                        pe.wait_ge(x_ready, CH)
                    for r in range(RB):
                        last = nc.tensor.matmul(m0[:, F * r:F * (r + 1)], closed[:, P * r:P * (r + 1)], fold,
                                                start=True, stop=True)
                    last.then_inc(folded, 1)
                if stage == 3 and ch["pair"] is not None:
                    pe.wait_ge(scaled, f + 1)
                    for r in range(RB):
                        last = nc.tensor.transpose(m0[:, P * r:P * (r + 1)], z_pair(g)[:, P * r:P * (r + 1)], ident)
                    last.then_inc(z_tp, 1)

            pe.wait_ge(const_in, 16)
            for n, step in enumerate(steps):
                t = prologue(n, 3)
                if t is not None:
                    pe.wait_ge(h_ready, t + 1)
                    if t >= 1:
                        pe.wait_ge(x_ready, t)
                    for r in range(RB):
                        last = nc.tensor.transpose(m0[:, P * r:P * (r + 1)],
                                                   xc[:, 2 * r:2 * r + 2, :].rearrange("p b f -> p (b f)"), ident)
                    last.then_inc(ht_tp, 1)
                t = prologue(n, 4)
                if t is not None:
                    if t == 0:
                        pe.wait_ge(w_in, 32)
                    pe.wait_ge(ht_ready, t + 1)
                    for r in range(RB):
                        last = nc.tensor.matmul(m0[:, P * r:P * (r + 1)], h_t[:, P * r:P * (r + 1)], w2[:],
                                                start=True, stop=True)
                    last.then_inc(x_mm, 1)
                u = step["use"]
                if u is None:
                    continue
                for j in range(RB):
                    transposes(u, j)
                    v = RB * u["m"] + j - LAG
                    if v >= 0:
                        products(uses[v // RB], v % RB)
                for stage, ch in close_at.get(u["m"], ()):
                    close(stage, ch)
            for v in range(RB * n_uses - LAG, RB * n_uses):
                products(uses[v // RB], v % RB)
            for m in range(n_uses, n_uses + 3):
                for stage, ch in close_at.get(m, ()):
                    close(stage, ch)
            pe.wait_ge(mv_ready, 1)
            pe.wait_ge(z_copied, CH)
            nc.tensor.matmul(m0[:, 0:1], half, mv[:, 0:1], start=True, stop=True).then_inc(mean_mm, 1)
            pe.wait_ge(q_ready, 1)
            nc.tensor.matmul(m0[:, 0:1], half, fin[:, 1:2], start=True, stop=True).then_inc(var_mm, 1)
            for t in range(CH):
                pe.wait_ge(act_done, t + 1)
                if t >= DEPTH:
                    pe.wait_ge(out_ready, t - DEPTH + 1)
                for r in range(RB):
                    every_fourth = z_pair(2 * t).rearrange("p (q i) -> p i q", i=RB)[:, r]
                    last = nc.tensor.transpose(tp[t % DEPTH][:, P * r:P * (r + 1)], every_fourth, ident)
                last.then_inc(out_tp, 1)

        @block.scalar
        def _(act):
            act.dma_start(cst[:], consts).then_inc(const_in, 16)
            act.wait_ge(w_zero, 1)
            act.dma_start(w2[0:F, 0:F], w).then_inc(w_in, 16)
            act.dma_start(w2[F:P, F:P], w).then_inc(w_in, 16)
            act.dma_start(bias[:], b.unsqueeze(0).to_broadcast([P, F])).then_inc(small_in, 16)
            for s, v in ((gam, gamma), (bet, beta)):
                for half_at in (0, F):
                    act.dma_start(s[half_at:half_at + F, :], v.unsqueeze(1)).then_inc(small_in, 16)

            def close(stage, ch):
                k, g = ch["k"], ch["g"]
                if stage == 1:
                    act.wait_ge(used, RB * (ch["uses"][-1]["m"] + 1))
                    if k >= 1:
                        act.wait_ge(folded, k)
                    nc.scalar.activation(closed[:], acc[ch["acc"]][:], ACT.Copy).then_inc(evacuated, 1)
                if stage == 3 and ch["pair"] is not None:
                    act.wait_ge(z_stat, ch["pair"] + 1)
                    nc.scalar.activation(z_pair(g), m0[:], ACT.Copy).then_inc(z_copied, 1)

            def round_hi(m, j):
                v = RB * m + j
                act.wait_ge(tp_ready, v + 1)
                if v >= DEPTH:
                    act.wait_ge(used, v - DEPTH + 1)
                nc.scalar.activation(hi[:, v % DEPTH, :], tp[v % DEPTH][:], ACT.Copy).then_inc(hi_ready, 1)

            def sum_rows(ld, r):
                g, c, nth = ld["g"], ld["c"], ld["sum"][1]
                if r == 0:
                    wait_load(act, ld)
                    if g >= 2:
                        act.wait_ge(deg_ready, g - 1)
                done = RB * (nth - 1) + r
                if done >= 2:
                    act.wait_ge(sums_a, done - 1)
                nc.scalar.activation(junk[:, r % 2, :], tile(ld["place"])[:, r, :], ACT.Copy,
                                           accum_out=rowsum[:, g % 2, r, c:c + 1]).then_inc(sums_a, 1)

            for n, step in enumerate(steps):
                u = step["use"]
                in_turn(step, "a", round_hi, sum_rows)
                t = prologue(n, 0)
                if t is not None:
                    act.wait_ge(xc_ready, t + 1)
                    nc.scalar.activation(sq, xc, ACT.Square).then_inc(sq_ready, 1)
                t = prologue(n, 3)
                if t is not None:
                    act.wait_ge(ht_tp, t + 1)
                    if t >= 1:
                        act.wait_ge(x_mm, t)
                    nc.scalar.activation(h_t.rearrange("p (q i) -> p i q", i=RB),
                                         m0[:].rearrange("p (i q) -> p i q", i=RB), ACT.Copy).then_inc(ht_ready, 1)
                if u is not None:
                    for stage, ch in close_at.get(u["m"], ()):
                        close(stage, ch)
            for m in range(n_uses, n_uses + 3):
                for stage, ch in close_at.get(m, ()):
                    close(stage, ch)
            act.wait_ge(ab_ready, 1)
            for t in range(CH):
                part = z[:, CB * F * t:CB * F * (t + 1)]
                nc.scalar.activation(part, part, ACT.Identity, bias=fin[:, 6:7],
                                     scale=fin[:, 5:6]).then_inc(affine, 1)

        @block.vector
        def _(dve):
            nc.vector.memset(w2[:], 0.0).then_inc(w_zero, 1)
            own = [0]

            def link(ins):
                own[0] += 1
                ins.then_inc(v_step, 1)
                dve.wait_ge(v_step, own[0])

            def close(stage, ch):
                k, g, f = ch["k"], ch["g"], ch["final"]
                if stage == 2:
                    dve.wait_ge(folded, k + 1)
                    rows = z_pair(g).rearrange("p (r h f) -> p r h f", h=2, f=F)[:, :, g % 2]
                    new = m0[:, 0:2 * P].rearrange("p (r f) -> p r f", f=F)
                    if ch["opens"]:
                        ins = nc.vector.tensor_copy(rows, new)
                    else:
                        ins = nc.vector.tensor_tensor(rows, new, rows, ALU.add)
                    ins.then_inc(combined, 1)
                    if f is not None:
                        dve.wait_ge(combined, k + 1)
                        dve.wait_ge(dinv_ready, g + 1)
                        nc.vector.tensor_tensor(rows, rows, dinv[:, g].unsqueeze(2).to_broadcast([P, RB, F]),
                                                ALU.mult).then_inc(scaled, 1)
                if stage == 3 and ch["pair"] is not None:
                    dve.wait_ge(z_tp, ch["pair"] + 1)
                    nc.vector.bn_stats(stats[:, ch["pair"], :], m0[:]).then_inc(z_stat, 1)

            def take_lo(m, j):
                v = RB * m + j
                dve.wait_ge(hi_ready, v + 1)
                if v >= DEPTH:
                    dve.wait_ge(used, v - DEPTH + 1)
                nc.vector.tensor_tensor(lo[:, v % DEPTH, :], tp[v % DEPTH][:], hi[:, v % DEPTH, :].bitcast(fp32),
                                        ALU.subtract).then_inc(lo_ready, 1)

            def sum_rows(ld, r):
                if r == 0:
                    wait_load(dve, ld)
                at = rowsum[:, ld["g"] % 2, r, ld["c"]:ld["c"] + 1]
                ins = nc.vector.tensor_reduce(at, tile(ld["place"])[:, r, :], AX.X, ALU.add)
                if r == RB - 1:
                    ins.then_inc(sums_v, 1)

            for n, step in enumerate(steps):
                u, g, c = step["use"], step["g"], step["c"]
                in_turn(step, "v", take_lo, sum_rows)
                if step["kind"] == "diag":
                    wait_load(dve, step["load"])
                    for r in range(RB):
                        at = diag[:, r, P * r:P * (r + 1)]
                        last = nc.vector.tensor_tensor(at, at, ident, ALU.add)
                    last.then_inc(diag_ready, 1)
                    dve.wait_ge(diag_ready, g + 1)
                    nc.vector.tensor_reduce(rowsum[:, g % 2, :, c:c + 1], diag[:], AX.X, ALU.add).then_inc(sums_v, 1)
                    dve.wait_ge(sums_v, step["load"]["sum"][1])
                    dve.wait_ge(sums_a, RB * step["sums_a"])
                    nc.vector.tensor_reduce(deg[:, g].unsqueeze(2), rowsum[:, g % 2], AX.X, ALU.add).then_inc(deg_ready, 1)
                t = prologue(n, 0)
                if t is not None:
                    xs = z[:, CB * F * t:CB * F * (t + 1)].rearrange("p (b f) -> p b f", f=F)
                    if t == 0:
                        dve.wait_ge(x_in, 16)
                        dve.wait_ge(const_in, 16)
                        dve.wait_ge(small_in, 80)
                    else:
                        dve.wait_ge(ht_tp, t)
                    link(nc.vector.tensor_reduce(mean[:].unsqueeze(2), xs, AX.X, ALU.add))
                    link(nc.vector.tensor_scalar(mean[:], mean[:], 1.0 / F, None, ALU.mult))
                    nc.vector.tensor_tensor(xc.rearrange("p (i h) f -> p h i f", h=2),
                                            xs.rearrange("p (h i) f -> p h i f", h=2),
                                            mean[:].rearrange("p (h i) -> p h i", h=2).unsqueeze(3).to_broadcast(
                                                [P, 2, RB, F]), ALU.subtract).then_inc(xc_ready, 1)
                t = prologue(n, 1)
                if t is not None:
                    dve.wait_ge(sq_ready, t + 1)
                    link(nc.vector.tensor_reduce(var[:].unsqueeze(2), sq, AX.X, ALU.add))
                    nc.vector.tensor_scalar(var[:], var[:], 1.0 / F, LN_EPS, ALU.mult, ALU.add).then_inc(var_ready, 1)
                t = prologue(n, 2)
                if t is not None:
                    dve.wait_ge(rstd_ready, t + 1)
                    link(nc.vector.tensor_scalar(xc, xc, 0.0, None, ALU.max))
                    nc.vector.tensor_tensor(xc, xc, rstd[:].unsqueeze(2).to_broadcast([P, CB, F]),
                                            ALU.mult).then_inc(h_ready, 1)
                t = prologue(n, 5)
                if t is not None:
                    dve.wait_ge(x_mm, t + 1)
                    nc.vector.tensor_tensor(y[:, CB * t:CB * (t + 1), :].rearrange("p (h r) f -> p h r f", h=2),
                                            m0[:].rearrange("p (r h f) -> p h r f", h=2, f=F),
                                            bias[:].unsqueeze(1).unsqueeze(1).to_broadcast([P, 2, RB, F]),
                                            ALU.add).then_inc(x_ready, 1)
                if u is not None:
                    for stage, ch in close_at.get(u["m"], ()):
                        close(stage, ch)
            for m in range(n_uses, n_uses + 3):
                for stage, ch in close_at.get(m, ()):
                    close(stage, ch)
            dve.wait_ge(z_stat, CH)
            nc.vector.bn_aggr(mv[:], stats[:].rearrange("p g s -> p (g s)")).then_inc(mv_ready, 1)
            dve.wait_ge(mean_mm, 1)
            dve.wait_ge(mv_ready, 1)
            link(nc.vector.tensor_copy(fin[:, 4:5], m0[:, 0:1]))
            link(nc.vector.tensor_tensor(fin[:, 0:1], mv[:, 0:1], fin[:, 4:5], ALU.subtract))
            link(nc.vector.tensor_tensor(fin[:, 1:2], fin[:, 0:1], fin[:, 0:1], ALU.mult))
            nc.vector.tensor_tensor(fin[:, 1:2], fin[:, 1:2], mv[:, 1:2], ALU.add).then_inc(q_ready, 1)
            dve.wait_ge(var_mm, 1)
            nc.vector.tensor_scalar(fin[:, 2:3], m0[:, 0:1], BN_EPS, None, ALU.add).then_inc(bnv_ready, 1)
            dve.wait_ge(bnr_ready, 1)
            link(nc.vector.tensor_tensor(fin[:, 5:6], fin[:, 3:4], gam[:], ALU.mult))
            link(nc.vector.tensor_tensor(fin[:, 7:8], fin[:, 4:5], fin[:, 5:6], ALU.mult))
            nc.vector.tensor_tensor(fin[:, 6:7], bet[:], fin[:, 7:8], ALU.subtract).then_inc(ab_ready, 1)

            def leaky(t):
                dve.wait_ge(affine, t + 1)
                part = z[:, CB * F * t:CB * F * (t + 1)]
                nc.vector.scalar_tensor_tensor(part, part, SLOPE, part, ALU.mult, ALU.max).then_inc(act_done, 1)

            leaky(0)
            dve.wait_ge(xl_in, 16)
            for t in range(CH):
                if t + 1 < CH:
                    leaky(t + 1)
                dve.wait_ge(out_tp, t + 1)
                nc.vector.tensor_tensor(tail_o[:, t].rearrange("p h (i f) -> p h i f", f=F),
                                        tp[t % DEPTH][:].rearrange("p (i h f) -> p h i f", h=2, f=F),
                                        tail_x[:, t].rearrange("p h (i f) -> p h i f", f=F),
                                        ALU.add).then_inc(out_ready, 1)


def kernel(x, adj, L0_gnn_W, L0_gnn_b, L0_gnn_gamma, L0_gnn_beta):
    import numpy as np
    import concourse.bacc as bacc
    from concourse.bass_utils import run_bass_kernel_spmd

    eye = np.eye(P, dtype=np.float32)
    same = np.tile(np.eye(F, dtype=np.float32), (2, 1))
    consts = np.concatenate([eye, 0.5 * np.tile(same, (1, 2)), same], axis=1)
    arrays = {"x": x, "adj": adj, "w": L0_gnn_W, "b": L0_gnn_b, "gamma": L0_gnn_gamma, "beta": L0_gnn_beta,
              "consts": consts}
    arrays = {f"{k}_dram": np.ascontiguousarray(v) for k, v in arrays.items()}
    nc = bacc.Bacc("TRN2", target_bir_lowering=False, num_devices=1)
    args = [nc.dram_tensor(k, v.shape, mybir.dt.from_np(v.dtype), kind="ExternalInput").ap()
            for k, v in arrays.items()]
    out = nc.dram_tensor("out_dram", (N, F), mybir.dt.float32, kind="ExternalOutput").ap()
    layer_kernel(nc, *args, out)
    return run_bass_kernel_spmd(nc, [arrays], core_ids=[0]).results[0]["out_dram"]
```
